# Optimizing a Trainium2 kernel written in Bass

```python
import numpy as np
import jax
import jax.numpy as jnp

def _softmax(x, axis=-1):
    return jax.nn.softmax(x, axis=axis)

def _gelu(x):
    return jax.nn.gelu(x, approximate=True)

def _silu(x):
    return jax.nn.silu(x)

def _sigmoid(x):
    return jax.nn.sigmoid(x)

def _layernorm(x, axis=-1, eps=1e-05):
    m = jnp.mean(x, axis=axis, keepdims=True)
    v = jnp.var(x, axis=axis, keepdims=True)
    return (x - m) / jnp.sqrt(v + eps)

def _scatter_add(tgt, idx, src, axis=0):
    return tgt.at[idx].add(src)

def _segment_sum(src, seg, n):
    return jax.ops.segment_sum(src, seg, n)
kernel_name = 'mk_gnn_ffn_d1_gnn_r8_1cf42a'

def setup_inputs(seed: int=0):
    np.random.seed(seed)
    _w = jnp.asarray

    def _rec_inputs():
        import jax
        import jax.numpy as jnp
        _gk = jax.random.key(seed)
        x = -0.0002117 + 1 * jax.random.normal(jax.random.fold_in(_gk, 1), (6250, 256), jnp.float32)
        src = jax.random.randint(jax.random.fold_in(_gk, 2), (200000,), 0, 6250, jnp.int32)
        dst = jnp.minimum((6250 * jax.random.uniform(jax.random.fold_in(_gk, 3), (200000,)) ** 2.0).astype(jnp.int32), 49999)
        _o = jnp.argsort(dst, stable=True)
        src = src[_o]
        dst = dst[_o]
        edge_attr_2 = jax.random.uniform(jax.random.fold_in(_gk, 11), (200000, 2), jnp.float32, 0.0, 1)
        return (x, src, dst, edge_attr_2)
    x, src, dst, edge_attr_2 = _rec_inputs()

    def _L0_gnn_setup():
        import jax, jax.numpy as jnp
        import numpy as np
        N_NODES = 12500
        N_EDGES = 200000
        IN_FEATS = 256
        OUT_FEATS = 64
        NUM_HEADS = 4
        key = jax.random.key(seed)
        k_h, k_adj, k_dir, k_wf, k_wr, k_af = jax.random.split(key, 6)
        h = jax.random.normal(k_h, (N_NODES, IN_FEATS), dtype=jnp.float32)
        adj = jax.random.randint(k_adj, (2, N_EDGES), 0, N_NODES, dtype=jnp.int64)
        bit = jax.random.randint(k_dir, (N_EDGES,), 0, 2).astype(jnp.float32)
        direction = jnp.stack([bit, 1.0 - bit], axis=1)
        s_w = float(np.sqrt(6.0 / (IN_FEATS + OUT_FEATS)))
        s_a = float(np.sqrt(6.0 / (NUM_HEADS + OUT_FEATS)))
        W_forward = jax.random.uniform(k_wf, (OUT_FEATS, IN_FEATS), jnp.float32, -s_w, s_w)
        W_reverse = jax.random.uniform(k_wr, (OUT_FEATS, IN_FEATS), jnp.float32, -s_w, s_w)
        attn_forward = jax.random.uniform(k_af, (1, NUM_HEADS, OUT_FEATS), jnp.float32, -s_a, s_a)
        return {'h': h, 'adj': adj, 'direction': direction, 'W_forward': W_forward, 'W_reverse': W_reverse, 'attn_forward': attn_forward}
    _L0_gnn_all = _L0_gnn_setup()
    _L0_gnn_in = {k: v for k, v in _L0_gnn_all.items() if k in ('W_forward', 'W_reverse', 'attn_forward')}
    del _L0_gnn_all

    def _L0_ffn_setup():
        import jax, jax.numpy as jnp
        import numpy as np
        B, T, D, H, E = (16, 512, 256, 512, 8)
        key = jax.random.key(seed)
        ks = jax.random.split(key, 5)
        x = jax.random.normal(ks[0], (B, T, D), dtype=jnp.float32)
        gate_w = jax.random.normal(ks[1], (D, E), dtype=jnp.float32) * 0.02
        gate_b = jnp.zeros((E,), dtype=jnp.float32)
        W1 = jax.random.normal(ks[2], (E, D, H), dtype=jnp.float32) * 0.02
        b1 = jnp.zeros((E, H), dtype=jnp.float32)
        W2 = jax.random.normal(ks[3], (E, H, D), dtype=jnp.float32) * 0.02
        b2 = jnp.zeros((E, D), dtype=jnp.float32)
        return {'x': x, 'gate_w': gate_w, 'gate_b': gate_b, 'W1': W1, 'b1': b1, 'W2': W2, 'b2': b2}
    _L0_ffn_all = _L0_ffn_setup()
    _L0_ffn_in = {k: v for k, v in _L0_ffn_all.items() if k in ('gate_w', 'gate_b', 'W1', 'b1', 'W2', 'b2')}
    del _L0_ffn_all
    return {'x': x, 'src': src, 'dst': dst, 'edge_attr_2': edge_attr_2, 'L0_gnn_W_forward': _L0_gnn_in['W_forward'], 'L0_gnn_W_reverse': _L0_gnn_in['W_reverse'], 'L0_gnn_attn_forward': _L0_gnn_in['attn_forward'], 'L0_ffn_gate_w': _L0_ffn_in['gate_w'], 'L0_ffn_gate_b': _L0_ffn_in['gate_b'], 'L0_ffn_W1': _L0_ffn_in['W1'], 'L0_ffn_b1': _L0_ffn_in['b1'], 'L0_ffn_W2': _L0_ffn_in['W2'], 'L0_ffn_b2': _L0_ffn_in['b2']}

def reference(x, src, dst, edge_attr_2, L0_gnn_W_forward, L0_gnn_W_reverse, L0_gnn_attn_forward, L0_ffn_gate_w, L0_ffn_gate_b, L0_ffn_W1, L0_ffn_b1, L0_ffn_W2, L0_ffn_b2):
    import jax
    import jax.numpy as jnp

    def _L0_gnn_ref(h, adj, direction, W_forward, W_reverse, attn_forward):
        import jax, jax.numpy as jnp
        import numpy as np
        N_NODES = 12500
        N_EDGES = 200000
        IN_FEATS = 256
        OUT_FEATS = 64
        NUM_HEADS = 4
        N = h.shape[0]
        H = attn_forward.shape[1]
        h_fwd = h @ W_forward.T
        h_rev = h @ W_reverse.T
        src, dst = (adj[0], adj[1])
        messages = h_fwd[src] * direction[:, 0:1] + h_rev[src] * direction[:, 1:2]
        scores = jnp.einsum('ef,hf->eh', messages, attn_forward[0])
        scores = jax.nn.leaky_relu(scores, negative_slope=0.2)
        exp_scores = jnp.exp(scores - scores.max(axis=0, keepdims=True))
        sum_exp = jax.ops.segment_sum(exp_scores, dst, num_segments=N)
        norm = exp_scores / (sum_exp[dst] + 1e-10)
        outs = [jax.ops.segment_sum(messages * norm[:, hd:hd + 1], dst, num_segments=N) for hd in range(H)]
        out = jnp.stack(outs, axis=1)
        return out.reshape(N, -1)

    def _L0_ffn_ref(x, gate_w, gate_b, W1, b1, W2, b2):
        import jax, jax.numpy as jnp
        import numpy as np
        B, T, D, H, E = (16, 512, 256, 512, 8)
        Bb, Tt, Dd = x.shape
        Ee = gate_w.shape[1]
        xf = x.reshape(-1, Dd)
        N = xf.shape[0]
        logits = xf @ gate_w + gate_b
        probs = jax.nn.softmax(logits, axis=-1)
        top2_vals, top2_idx = jax.lax.top_k(probs, 2)
        cw = jnp.zeros((N, Ee), dtype=xf.dtype).at[jnp.arange(N)[:, None], top2_idx].add(top2_vals)

        def step(acc, params):
            w1, bb1, w2, bb2, we = params
            h = jax.nn.gelu(xf @ w1 + bb1, approximate=False)
            y = h @ w2 + bb2
            return (acc + we[:, None] * y, None)
        out, _ = jax.lax.scan(step, jnp.zeros_like(xf), (W1, b1, W2, b2, cw.T))
        return out.reshape(Bb, Tt, Dd)
    edge_index = jnp.stack([src, dst])
    x = x + _L0_gnn_ref(_layernorm(x, axis=-1), edge_index, edge_attr_2, L0_gnn_W_forward, L0_gnn_W_reverse, L0_gnn_attn_forward)
    x = x + _L0_ffn_ref(_layernorm(x, axis=-1)[None], L0_ffn_gate_w, L0_ffn_gate_b, L0_ffn_W1, L0_ffn_b1, L0_ffn_W2, L0_ffn_b2)[0]
    return x

_drawn_inputs = setup_inputs


def setup_inputs(seed=0):
    import zlib

    import numpy as np

    out = dict(_drawn_inputs(seed))
    spreads = {'L0_ffn_gate_b': (0.0, 0.488), 'L0_ffn_b1': (0.0, 0.8), 'L0_ffn_b2': (0.0, 0.359)}
    factors = {'L0_ffn_W1': 3.277, 'L0_ffn_W2': 3.082}
    for name, (base, spread) in spreads.items():
        noise = np.random.default_rng([zlib.crc32(name.encode()), seed]).standard_normal(out[name].shape)
        drawn = base * np.exp(spread * noise) if base else spread * noise
        out[name] = jnp.asarray(drawn.astype(out[name].dtype))
    for name, factor in factors.items():
        out[name] = (out[name] * factor).astype(out[name].dtype)
    return out
```

```python
from contextlib import ExitStack

import concourse.bass as bass
from concourse import mybir

F32 = mybir.dt.float32
I32 = mybir.dt.int32
ALU = mybir.AluOpType
ACT = mybir.ActivationFunctionType
AX = mybir.AxisListType

P = 128
N_NODES, D = 6250, 256
N_EDGES = 200000
F, HEADS = 64, 4
HALF_ROW = F + HEADS
ROW = 2 * HALF_ROW
HEAD_COLS = F + 1
ACC = HEADS * HEAD_COLS
TILES = 8
GROUP = TILES * P
N_GROUPS = -(-N_EDGES // GROUP)
HALF_GROUPS = N_GROUPS // 2
TAIL = N_EDGES - (N_GROUPS - 1) * GROUP
N_FULL = N_NODES // P
LAST = N_NODES - N_FULL * P
N_BLOCKS = N_FULL + 2
EXPERTS, HID = 8, 512
D_CHUNKS, H_CHUNKS = D // P, HID // P
SLOT_TILE = 256
SUB = SLOT_TILE // P
HID_BANKS = H_CHUNKS * SLOT_TILE // 512
N_SLOT_TILES = (2 * N_NODES + EXPERTS * (SLOT_TILE - 1)) // SLOT_TILE
N_SLOT_TILES += N_SLOT_TILES % 2
N_SLOTS = N_SLOT_TILES * SLOT_TILE
SCATTER_BUFS = 4
GUARD_CAP = 80.0
EPS = 1e-5
LEAK = 0.2
GUARD = 1e-10
LOWEST = -1e30
assert N_GROUPS % 2 == 0 and N_FULL % 4 == 0 and N_BLOCKS % 2 == 0

def at_least(engine, sem, value):
    if isinstance(value, int) and value <= 0:
        return
    engine.wait_ge(sem, value)

def cols(start, size):
    return slice(start, start + size) if isinstance(start, int) else bass.ds(start, size)

def build(nc, x, src, dst, edge_attr, w_fwd, w_rev, attn, gate_w, gate_b, w1, b1, w2, b2, out):
    table = nc.dram_tensor("node_table", (N_BLOCKS * P, ROW), F32, kind="Internal").ap()
    slots_in = nc.dram_tensor("slots_in", (N_SLOTS, D), F32, kind="Internal").ap()
    slots_out = nc.dram_tensor("slots_out", (N_SLOTS, D), F32, kind="Internal").ap()

    with ExitStack() as ctx:
        def sb(name, shape, dt=F32):
            return ctx.enter_context(nc.sbuf_tensor(name, shape, dt))

        def sem(name):
            return ctx.enter_context(nc.semaphore(name))

        xres = sb("xres", [P, N_BLOCKS * D])
        acc = sb("acc", [P, N_BLOCKS * ACC])
        src_t = sb("src_t", [P, (N_GROUPS + 2) * TILES], I32)
        dst_t = sb("dst_t", [P, N_GROUPS * TILES])
        ea_t = sb("ea_t", [P, 2, N_GROUPS * TILES])
        ident = sb("ident", [P, P])
        iota0 = sb("iota0", [P, P])
        iota1 = sb("iota1", [P, P])
        ones = sb("ones", [P, P])
        upper = sb("upper", [P, P])
        stats = sb("stats", [P, N_BLOCKS, 6])
        mean = sb("mean", [P, N_BLOCKS])
        rstd = sb("rstd", [P, N_BLOCKS])
        ln_a = sb("ln_a", [P, N_BLOCKS])
        ln_b = sb("ln_b", [P, N_BLOCKS])
        eps_t = sb("eps_t", [P, 1])
        wcat = sb("wcat", [P, D_CHUNKS, ROW])
        attn_n = sb("attn_n", [HEADS, F])
        attn_t = sb("attn_t", [F, HEADS])
        gw = sb("gw", [P, D_CHUNKS, EXPERTS])
        gb = sb("gb", [P, EXPERTS])
        b1_n = sb("b1_n", [EXPERTS * H_CHUNKS, P])
        b1_t = sb("b1_t", [P, EXPERTS * H_CHUNKS])
        blk_i = sb("blk_i", [HALF_GROUPS, 4], I32)
        blk_f = sb("blk_f", [HALF_GROUPS, 4])
        blk_row = sb("blk_row", [1, 2 * N_GROUPS])
        scan = sb("scan", [1, 2, N_GROUPS])
        walk = sb("walk", [1, 3, N_GROUPS], I32)
        m_all = sb("m_all", [P, N_GROUPS, HEADS])
        m_blk = sb("m_blk", [P, N_BLOCKS, HEADS])
        m_dif = sb("m_dif", [P, N_BLOCKS, HEADS])
        alpha = sb("alpha", [P, N_BLOCKS, HEADS])
        den = sb("den", [P, N_BLOCKS, HEADS])
        valid = sb("valid", [P, 1])
        zeros = sb("zeros", [P, D])
        col = sb("col", [P, 3, N_BLOCKS])
        weight = sb("weight", [P, 2, N_BLOCKS])
        slot_i = sb("slot_i", [P, N_BLOCKS, 2], I32)
        slot_u = sb("slot_u", [P, SCATTER_BUFS, 2], I32)
        counts = sb("counts", [P, 4, EXPERTS])
        count_i = sb("count_i", [P, EXPERTS], I32)
        tile_e = sb("tile_e", [1, N_SLOT_TILES])
        tile_i = sb("tile_i", [1, N_SLOT_TILES], I32)
        cur = sb("cur", [P, 2, TILES], I32)
        gmax = sb("gmax", [P, 2, HEADS])
        tmax = sb("tmax", [HEADS, 1])
        rmax = sb("rmax", [HEADS, 2])
        diag = sb("diag", [HEADS, 2, HEADS])
        xn = sb("xn", [P, 2, D])
        xn_t = sb("xn_t", [P, 2, D])
        row_o = sb("row_o", [P, 2, ROW])

        W = 13904
        work = sb("work", [P, W])
        used = [0]

        def carve(n, shape=None, dt=F32, parts=P):
            a = work[0:parts, used[0]:used[0] + n]
            used[0] += n
            assert used[0] <= W
            if dt is not F32:
                a = a.bitcast(dt)
            return a

        src_n = carve(2 * GROUP, dt=I32)
        dst_n = carve(2 * GROUP, dt=I32)
        ea_n = carve(4 * GROUP)
        src_f = carve(2 * GROUP)
        dst_f = carve(2 * GROUP)
        w_nat = carve(2 * D, parts=F).rearrange("p (k d) -> p k d", k=2)

        used[0] = 0
        rows = carve(2 * TILES * ROW).rearrange("p (u j r) -> p u j r", u=2, j=TILES)
        prod = carve(2 * TILES * ROW).rearrange("p (u j r) -> p u j r", u=2, j=TILES)
        msg = carve(2 * TILES * HALF_ROW).rearrange("p (u j r) -> p u j r", u=2, j=TILES)
        lrelu = carve(2 * TILES * HEADS).rearrange("p (u j h) -> p u j h", u=2, j=TILES)
        shifted = carve(2 * TILES * HEADS).rearrange("p (u j h) -> p u j h", u=2, j=TILES)
        wgt = carve(2 * TILES * HEADS).rearrange("p (u j h) -> p u j h", u=2, j=TILES)
        val = carve(2 * TILES * ACC).rearrange("p (u j c) -> p u j c", u=2, j=TILES)
        onehot = carve(2 * TILES * P).rearrange("p (u j n) -> p u j n", u=2, j=TILES)
        onehot_x = carve(2 * TILES * P).rearrange("p (u j n) -> p u j n", u=2, j=TILES)
        dst_k = carve(TILES)

        used[0] = 0
        b2_rep = carve(EXPERTS * D)
        tok = carve(SCATTER_BUFS * D).rearrange("p (u d) -> p u d", u=SCATTER_BUFS)
        y_tok = carve(2 * 2 * D).rearrange("p (u k d) -> p u k d", u=2, k=2)
        res = carve(2 * D).rearrange("p (u d) -> p u d", u=2)
        ffn_start = used[0]
        w1_s = carve(2 * D_CHUNKS * HID).rearrange("p (u c h) -> p u c h", u=2, c=D_CHUNKS)
        w2_s = carve(2 * H_CHUNKS * D).rearrange("p (u c d) -> p u c d", u=2, c=H_CHUNKS)
        x_in = carve(2 * SUB * D).rearrange("p (u s d) -> p u s d", u=2, s=SUB)
        x_int = carve(2 * D_CHUNKS * SLOT_TILE).rearrange("p (u k) -> p u k", u=2)
        hid = carve(2 * H_CHUNKS * SLOT_TILE).rearrange("p (u c k) -> p u c k", u=2, c=H_CHUNKS)
        y_out = carve(2 * SUB * D).rearrange("p (u k) -> p u k", u=2)
        used[0] = ffn_start
        BE = N_BLOCKS * EXPERTS

        def carve_be():
            return carve(BE).rearrange("p (t e) -> p t e", e=EXPERTS)

        prob, tmp_a, tmp_b, top_1, top_2, both, scan_a, scan_b, iota8 = (carve_be() for _ in range(9))
        tile_x = carve(N_SLOT_TILES * (EXPERTS - 1), parts=1).rearrange("p (t e) -> p t e", e=EXPERTS - 1)

        bank = [ctx.enter_context(nc.psum_tensor(f"bank{i}", [P, 512], F32)) for i in range(8)]

        x_loaded, x_tail_loaded, x_pad, w_loaded, src_loaded, dst_loaded, ea_loaded = map(
            sem, ["x_loaded", "x_tail_loaded", "x_pad", "w_loaded", "src_loaded", "dst_loaded", "ea_loaded"])
        consts, wt_ps, wt_done, at_done = map(sem, ["consts", "wt_ps", "wt_done", "at_done"])
        dst_conv, src_conv, tr_ps, tr_done = map(sem, ["dst_conv", "src_conv", "tr_ps", "tr_done"])
        blk_ready, blkrow_ps, blk_rep, walk_ready, setup_link = map(
            sem, ["blk_ready", "blkrow_ps", "blk_rep", "walk_ready", "setup_link"])
        row_first, edges_ready = map(sem, ["row_first", "edges_ready"])
        ln_link, ln_var, ln_std = map(sem, ["ln_link", "ln_var", "ln_std"])
        xn_ready, xnt_ps, xnt_ready, row_ps, row_ready = map(
            sem, ["xn_ready", "xnt_ps", "xnt_ready", "row_ps", "row_ready"])
        row_stored = [sem("row_stored0"), sem("row_stored1")]
        idx_ready = sem("idx_ready")
        gathered = [sem("gathered0"), sem("gathered1")]
        prod_ready, msg_ready, gmax_ready, gmaxt_ready, diag_ready, max_ready, msg_link = map(
            sem, ["prod_ready", "msg_ready", "gmax_ready", "gmaxt_ready", "diag_ready", "max_ready", "msg_link"])
        shifted_ready, wgt_ready, val_ready, sums_ready, dif_ready, alpha_ready = map(
            sem, ["shifted_ready", "wgt_ready", "val_ready", "sums_ready", "dif_ready", "alpha_ready"])
        max_link, acc_link, rest_ready, rest_sums, acc_zero = map(
            sem, ["max_link", "acc_link", "rest_ready", "rest_sums", "acc_zero"])
        edges_done, b2_loaded, guard_dif, guard_ready, gate_ps, logit_ready = map(
            sem, ["edges_done", "b2_loaded", "guard_dif", "guard_ready", "gate_ps", "logit_ready"])
        exp_in, exp_out, both_ready, rank_ps, plan_ready = map(
            sem, ["exp_in", "exp_out", "both_ready", "rank_ps", "plan_ready"])
        tok_ready, slot_copied, slots_zero, pool_step = map(sem, ["tok_ready", "slot_copied", "slots_zero", "pool_step"])
        scattered = [sem(f"scattered{i}") for i in range(SCATTER_BUFS)]
        w1_loaded, w2_loaded, xin_loaded, y_stored, y_fetched, res_stored = (
            [sem(f"{n}{i}") for i in range(2)] for n in
            ("w1_loaded", "w2_loaded", "xin_loaded", "y_stored", "y_fetched", "res_stored"))
        xin_ps, xin_ready, hid_ps, hid_ready, y_ps, y_ready, res_ready, res_link, fetch_idx = map(
            sem, ["xin_ps", "xin_ready", "hid_ps", "hid_ready", "y_ps", "y_ready", "res_ready", "res_link", "fetch_idx"])

        pool_turn = sem("pool_turn")
        block = ctx.enter_context(nc.Block())

        def bc(ap, shape):
            return ap.to_broadcast(shape)

        turned = [(src_f, src_t[:, 0:N_GROUPS * TILES]), (dst_f, dst_t[:, :]),
                  (ea_n.rearrange("p (c k) -> p k c", k=2)[:, 0, :], ea_t[:, 0, :]),
                  (ea_n.rearrange("p (c k) -> p k c", k=2)[:, 1, :], ea_t[:, 1, :])]
        turn_ready = [(src_conv, 1), (dst_conv, 1), (ea_loaded, 64), (ea_loaded, 64)]
        TURNS = len(turned) * 2 * 2

        @block.sync
        def _(sp):
            sp.dma_start(xres[:, 0:N_FULL * D].rearrange("p (t d) -> p t d", d=D),
                         x[0:N_FULL * P, :].rearrange("(t p) d -> p t d", p=P)).then_inc(x_loaded, 16)
            whole = (N_GROUPS - 1) * GROUP
            for sb_t, dram, signal, again in ((dst_n, dst, dst_loaded, N_EDGES - (GROUP - TAIL)),
                                              (src_n, src, src_loaded, 0)):
                cut = HALF_GROUPS * GROUP
                sp.dma_start(sb_t[0:HALF_GROUPS, 0:GROUP],
                             dram[0:cut].rearrange("(r c) -> r c", c=GROUP)).then_inc(signal, 16)
                sp.dma_start(sb_t[0:HALF_GROUPS - 1, GROUP:2 * GROUP],
                             dram[cut:whole].rearrange("(r c) -> r c", c=GROUP)).then_inc(signal, 16)
                sp.dma_start(sb_t[HALF_GROUPS - 1:HALF_GROUPS, GROUP:GROUP + TAIL],
                             dram[whole:N_EDGES].rearrange("(r c) -> r c", r=1)).then_inc(signal, 16)
                sp.dma_start(sb_t[HALF_GROUPS - 1:HALF_GROUPS, GROUP + TAIL:2 * GROUP],
                             dram[again:again + GROUP - TAIL].rearrange("(r c) -> r c", r=1)).then_inc(signal, 16)
            cut = HALF_GROUPS * GROUP
            sp.dma_start(ea_n[0:HALF_GROUPS, 0:2 * GROUP],
                         edge_attr[0:cut, :].rearrange("(r c) k -> r (c k)", c=GROUP)).then_inc(ea_loaded, 16)
            sp.dma_start(ea_n[0:HALF_GROUPS - 1, 2 * GROUP:4 * GROUP],
                         edge_attr[cut:whole, :].rearrange("(r c) k -> r (c k)", c=GROUP)).then_inc(ea_loaded, 16)
            sp.dma_start(ea_n[HALF_GROUPS - 1:HALF_GROUPS, 2 * GROUP:2 * GROUP + 2 * TAIL],
                         edge_attr[whole:N_EDGES, :].rearrange("(r c) k -> r (c k)", r=1)).then_inc(ea_loaded, 16)
            sp.dma_start(ea_n[HALF_GROUPS - 1:HALF_GROUPS, 2 * GROUP + 2 * TAIL:4 * GROUP],
                         edge_attr[0:GROUP - TAIL, :].rearrange("(r c) k -> r (c k)", r=1)).then_inc(ea_loaded, 16)

            def store_row(t, u, k):
                sp.wait_ge(row_ready, t + 1)
                sp.dma_start(table[cols(t * P, P), :], row_o[:, u, :]).then_inc(row_stored[u], 16)

            with sp.Fori(0, N_BLOCKS // 2) as k:
                for u in range(2):
                    store_row(2 * k + u, u, k)

            sp.wait_ge(consts, 2)
            sp.dma_start(slots_in.rearrange("(q p) d -> p q d", p=P),
                         zeros[:].unsqueeze(1).to_broadcast([P, N_SLOTS // P, D])).then_inc(slots_zero, 16)
            sp.wait_ge(edges_done, 1)
            sp.dma_start(b2_rep, b2.rearrange("(o e) d -> o (e d)", o=1).to_broadcast([P, EXPERTS * D])).then_inc(b2_loaded, 16)

            def load_tile(t, u, k):
                e = sp.value_load(tile_i[0:1, cols(t, 1)], min_val=0, max_val=EXPERTS - 1)
                at_least(sp, xin_ps, t - 1)
                sp.dma_start(x_in[:, u], slots_in[cols(t * SLOT_TILE, SLOT_TILE), :].rearrange("(s p) d -> p s d", p=P)
                             ).then_inc(xin_loaded[u], 16)
                at_least(sp, hid_ps, (t - 1) * HID_BANKS)
                sp.dma_start(w1_s[:, u], w1[cols(e, 1)].rearrange("o (c p) h -> p (o c) h", p=P)).then_inc(w1_loaded[u], 16)
                at_least(sp, y_ps, t - 1)
                sp.dma_start(w2_s[:, u], w2[cols(e, 1)].rearrange("o (c p) d -> p (o c) d", p=P)).then_inc(w2_loaded[u], 16)

            sp.wait_ge(plan_ready, 1)
            for q in range(SCATTER_BUFS):
                sp.wait_ge(scattered[q], 32 * (N_FULL // SCATTER_BUFS + (q == 0)))
            for t in range(2):
                load_tile(t, t, 0)
            with sp.Fori(1, N_SLOT_TILES // 2) as k:
                for u in range(2):
                    load_tile(2 * k + u, u, k)

            def store_result(t, u, rows_n=P):
                sp.wait_ge(res_ready, t + 1)
                sp.dma_start(out[cols(t * P, rows_n), :], res[0:rows_n, u, :]).then_inc(res_stored[u], 16)

            with sp.Fori(0, N_FULL // 2) as k:
                for u in range(2):
                    store_result(2 * k + u, u)
            store_result(N_FULL, 0, LAST)
            sp.wait_ge(res_stored[0], 16 * (N_FULL // 2 + 1))
            sp.wait_ge(res_stored[1], 16 * (N_FULL // 2))

        @block.gpsimd
        def _(pool):
            nc.gpsimd.memset(xres[:, N_FULL * D:], 0.0).then_inc(x_pad, 1)
            pool.wait_ge(x_pad, 1)
            pool.dma_start(xres[0:LAST, N_FULL * D:(N_FULL + 1) * D], x[N_FULL * P:N_NODES, :]).then_inc(x_tail_loaded, 16)
            pool.dma_start(w_nat[:, 0, :], w_fwd).then_inc(w_loaded, 16)
            pool.dma_start(w_nat[:, 1, :], w_rev).then_inc(w_loaded, 16)
            pool.dma_start(attn_n[:], attn.rearrange("o h f -> (o h) f")).then_inc(w_loaded, 16)
            pool.dma_start(gw[:], gate_w.rearrange("(c p) e -> p c e", p=P)).then_inc(w_loaded, 16)
            pool.dma_start(gb[:], gate_b.rearrange("(o e) -> o e", o=1).to_broadcast([P, EXPERTS])).then_inc(w_loaded, 16)
            pool.dma_start(b1_n[:], b1.rearrange("e (c p) -> (e c) p", p=P)).then_inc(w_loaded, 16)
            nc.gpsimd.memset(ident[:], 0.0)
            nc.gpsimd.memset(ones[:], 1.0)
            nc.gpsimd.memset(eps_t[:], EPS)
            nc.gpsimd.memset(zeros[:], 0.0)
            nc.gpsimd.iota(iota0[:], pattern=[[1, P]], base=0, channel_multiplier=0, allow_small_or_imprecise_dtypes=True)
            nc.gpsimd.iota(iota1[:], pattern=[[1, P]], base=P, channel_multiplier=0, allow_small_or_imprecise_dtypes=True)
            nc.gpsimd.memset(src_t[:, N_GROUPS * TILES:], 0.0).then_inc(consts, 1)
            pool.wait_ge(consts, 1)
            nc.gpsimd.affine_select(out=ident[:], in_=ident[:], compare_op=ALU.not_equal, fill=1.0, base=0,
                                    pattern=[[1, P]], channel_multiplier=-1)
            nc.gpsimd.affine_select(out=upper[:], in_=ones[:], compare_op=ALU.is_gt, fill=0.0, base=0,
                                    pattern=[[1, P]], channel_multiplier=-1)
            nc.gpsimd.affine_select(out=valid[:], in_=ones[:, 0:1], compare_op=ALU.is_gt, fill=0.0, base=LAST,
                                    pattern=[[0, 1]], channel_multiplier=-1).then_inc(consts, 1)

            def gather(g, u):
                at_least(pool, prod_ready, g - 1)
                pool.wait_ge(idx_ready, g + 1)
                pool.sem_inc(pool_turn, 1)
                for j in range(TILES):
                    nc.gpsimd.indirect_dma_start(
                        out=rows[:, u, j, :], out_offset=None, in_=table,
                        in_offset=bass.IndirectOffsetOnAxis(ap=cur[:, u, j:j + 1], axis=0)).then_inc(gathered[u], 16)

            pool.wait_ge(row_stored[0], 16 * (N_BLOCKS // 2))
            pool.wait_ge(row_stored[1], 16 * (N_BLOCKS // 2))
            pool.wait_ge(tr_done, TURNS)
            for g in range(2):
                gather(g, g % 2)
            with pool.Fori(1, N_GROUPS // 2) as k:
                for u in range(2):
                    gather(2 * k + u, u)

            def scatter(t, q, n=P):
                pool.wait_ge(tok_ready, t + 1)
                pool.wait_ge(slot_copied, t + 1)
                pool.sem_inc(pool_step, 1)
                for k in range(2):
                    nc.gpsimd.indirect_dma_start(
                        out=slots_in, out_offset=bass.IndirectOffsetOnAxis(ap=slot_u[0:n, q, k:k + 1], axis=0),
                        in_=tok[0:n, q, :], in_offset=None).then_inc(scattered[q], 16)

            pool.wait_ge(slots_zero, 16)
            for t in range(SCATTER_BUFS):
                scatter(t, t)
            with pool.Fori(1, N_FULL // SCATTER_BUFS) as k:
                for q in range(SCATTER_BUFS):
                    scatter(SCATTER_BUFS * k + q, q)
            scatter(N_FULL, 0, LAST)

            def fetch(t, u, n=P):
                pool.wait_ge(fetch_idx, t + 1)
                at_least(pool, res_ready, t - 1)
                pool.sem_inc(pool_step, 1)
                for k in range(2):
                    nc.gpsimd.indirect_dma_start(
                        out=y_tok[0:n, u, k, :], out_offset=None, in_=slots_out,
                        in_offset=bass.IndirectOffsetOnAxis(ap=slot_u[0:n, u, k:k + 1], axis=0)).then_inc(y_fetched[u], 16)

            for u in range(2):
                pool.wait_ge(y_stored[u], 16 * (N_SLOT_TILES // 2))
            for t in range(2):
                fetch(t, t)
            with pool.Fori(1, N_FULL // 2) as k:
                for u in range(2):
                    fetch(2 * k + u, u)
            fetch(N_FULL, 0, LAST)

        @block.tensor
        def _(pe):
            T = nc.tensor
            pe.wait_ge(consts, 2)
            pe.wait_ge(w_loaded, 96)
            for d in range(2):
                for c in range(D_CHUNKS):
                    T.transpose(bank[d][:, c * F:(c + 1) * F], w_nat[:, d, c * P:(c + 1) * P], ident[0:F, 0:F])
            T.transpose(bank[2][0:F, 0:HEADS], attn_n[:], ident[0:HEADS, 0:HEADS])
            nb1 = EXPERTS * H_CHUNKS
            T.transpose(bank[3][:, 0:nb1], b1_n[:], ident[0:nb1, 0:nb1]).then_inc(wt_ps, 1)
            pe.wait_ge(wt_done, 1)
            for d in range(2):
                for c in range(D_CHUNKS):
                    last = T.matmul(bank[4][:, (2 * d + c) * HEADS:(2 * d + c + 1) * HEADS],
                                    w_nat[:, d, c * P:(c + 1) * P], attn_t[:], start=True, stop=True)
            last.then_inc(wt_ps, 1)

            pe.wait_ge(blk_ready, 1)
            for q in range(4):
                last = T.transpose(bank[5][0:1, q * HALF_GROUPS:(q + 1) * HALF_GROUPS], blk_f[:, q:q + 1],
                                   ident[0:HALF_GROUPS, 0:HALF_GROUPS])
            last.then_inc(blkrow_ps, 1)
            pe.wait_ge(row_first, 1)
            T.matmul(bank[6][:, 0:N_GROUPS], ones[0:1, :], blk_row[0:1, 0:N_GROUPS], start=True, stop=True).then_inc(blkrow_ps, 1)

            n = 0
            pe.wait_ge(at_done, 1)
            for (source, _), (signal, count) in zip(turned, turn_ready):
                pe.wait_ge(signal, count)
                for half in range(2):
                    for q in range(2):
                        at_least(pe, tr_done, n - 1)
                        for j in range(4):
                            c0 = half * GROUP + (4 * q + j) * P
                            last = T.transpose(bank[n % 2][:, j * HALF_GROUPS:(j + 1) * HALF_GROUPS],
                                               source[0:HALF_GROUPS, c0:c0 + P], ident[0:HALF_GROUPS, 0:HALF_GROUPS])
                        last.then_inc(tr_ps, 1)
                        n += 1

            def turn_x(t, u, done=0):
                pe.wait_ge(xn_ready, done + t + 1)
                at_least(pe, xnt_ready, done + t - 1)
                for c in range(D_CHUNKS):
                    last = T.transpose(bank[2 + u][:, c * P:(c + 1) * P], xn[:, u, c * P:(c + 1) * P], ident[:])
                last.then_inc(xnt_ps, 1)

            def project(t, u):
                pe.wait_ge(xnt_ready, t + 1)
                at_least(pe, row_ready, t - 1)
                for c in range(D_CHUNKS):
                    last = T.matmul(bank[6 + u][:, 0:ROW], xn_t[:, u, c * P:(c + 1) * P], wcat[:, c, :],
                                    start=(c == 0), stop=(c == D_CHUNKS - 1))
                last.then_inc(row_ps, 1)

            pe.wait_ge(edges_ready, 1)
            pe.wait_ge(wt_done, 2)
            for t in range(2):
                turn_x(t, t)
            project(0, 0)
            with pe.Fori(1, N_BLOCKS // 2) as k:
                turn_x(2 * k, 0)
                project(2 * k - 1, 1)
                turn_x(2 * k + 1, 1)
                project(2 * k, 0)
            project(N_BLOCKS - 1, 1)

            def max_turn(g, u):
                pe.wait_ge(gmax_ready, g + 1)
                T.transpose(bank[4][0:HEADS, u * P:(u + 1) * P], gmax[:, u, :], ident[:]).then_inc(gmaxt_ready, 1)

            def max_spread(g, u):
                pe.wait_ge(diag_ready, g + 1)
                T.matmul(bank[5][:, u * HEADS:(u + 1) * HEADS], ones[0:HEADS, :], diag[:, u, :],
                         start=True, stop=True).then_inc(max_ready, 1)

            def sums(to, hot, u):
                for j in range(TILES):
                    last = T.matmul(to[:, 0:ACC], hot[:, u, j, :], val[:, u, j, :], start=(j == 0), stop=(j == TILES - 1))
                return last

            def group_sums(g, u):
                pe.wait_ge(val_ready, g + 1)
                more = pe.value_load(walk[0:1, 1, cols(g, 1)], min_val=0, max_val=N_BLOCKS)
                with pe.If(more > 0):
                    sums(bank[2 + u], onehot_x, u)
                sums(bank[u], onehot, u).then_inc(sums_ready, 1)

            def rest_of_blocks(g, u):
                more = pe.value_load(walk[0:1, 1, cols(g, 1)], min_val=0, max_val=N_BLOCKS)
                with pe.If(more > 1):
                    before = pe.value_load(walk[0:1, 2, cols(g, 1)], min_val=0, max_val=N_BLOCKS * N_GROUPS)
                    with pe.Fori(1, more) as k:
                        pe.wait_ge(rest_ready, before + k)
                        sums(bank[6], onehot_x, u).then_inc(rest_sums, 1)

            def slot(g, u, first=True, second=True, third=True):
                if first:
                    max_turn(g, u)
                    max_spread(g, u)
                if third:
                    rest_of_blocks(g - 2, u)
                if second:
                    group_sums(g - 1, 1 - u)

            pe.wait_ge(walk_ready, 1)
            slot(0, 0, second=False, third=False)
            slot(1, 1, third=False)
            with pe.Fori(1, N_GROUPS // 2) as k:
                for u in range(2):
                    slot(2 * k + u, u)
            slot(N_GROUPS, 0, first=False)
            slot(N_GROUPS + 1, 1, first=False, second=False)

            def gate(t, u):
                pe.wait_ge(xnt_ready, N_BLOCKS + t + 1)
                at_least(pe, logit_ready, t - 1)
                for c in range(D_CHUNKS):
                    last = T.matmul(bank[6 + u][:, 0:EXPERTS], xn_t[:, u, c * P:(c + 1) * P], gw[:, c, :],
                                    start=(c == 0), stop=(c == D_CHUNKS - 1))
                last.then_inc(gate_ps, 1)

            for t in range(2):
                turn_x(t, t, N_BLOCKS)
            gate(0, 0)
            with pe.Fori(1, N_BLOCKS // 2) as k:
                turn_x(2 * k, 0, N_BLOCKS)
                gate(2 * k - 1, 1)
                turn_x(2 * k + 1, 1, N_BLOCKS)
                gate(2 * k, 0)
            gate(N_BLOCKS - 1, 1)

            pe.wait_ge(both_ready, 1)
            flat = both.rearrange("p t e -> p (t e)")
            T.matmul(bank[0][:, 0:BE], upper[:], flat, start=True, stop=True)
            T.matmul(bank[1][:, 0:BE], ones[:], flat, start=True, stop=True).then_inc(rank_ps, 1)

            def turn_in(t, u, k):
                pe.wait_ge(xin_loaded[u], 16 * (k + 1))
                at_least(pe, xin_ready, t - 1)
                for c in range(D_CHUNKS):
                    for i in range(SUB):
                        last = T.transpose(bank[u][:, c * SLOT_TILE + i * P:c * SLOT_TILE + (i + 1) * P],
                                           x_in[:, u, i, c * P:(c + 1) * P], ident[:])
                last.then_inc(xin_ps, 1)

            def up(t, u, k):
                pe.wait_ge(xin_ready, t + 1)
                pe.wait_ge(w1_loaded[u], 16 * (k + 1))
                at_least(pe, hid_ready, H_CHUNKS * (t - 1))
                for c in range(H_CHUNKS):
                    for d in range(D_CHUNKS):
                        last = T.matmul(bank[2 + 2 * u + c // 2][:, (c % 2) * SLOT_TILE:(c % 2 + 1) * SLOT_TILE],
                                        w1_s[:, u, d, c * P:(c + 1) * P], x_int[:, u, d * SLOT_TILE:(d + 1) * SLOT_TILE],
                                        start=(d == 0), stop=(d == D_CHUNKS - 1))
                    if c % 2:
                        last.then_inc(hid_ps, 1)

            def down(t, u, k):
                pe.wait_ge(hid_ready, H_CHUNKS * (t + 1))
                pe.wait_ge(w2_loaded[u], 16 * (k + 1))
                at_least(pe, y_ready, t - 1)
                for i in range(SUB):
                    for c in range(H_CHUNKS):
                        last = T.matmul(bank[6 + u][:, i * D:(i + 1) * D], hid[:, u, c, i * P:(i + 1) * P], w2_s[:, u, c, :],
                                        start=(c == 0), stop=(c == H_CHUNKS - 1))
                last.then_inc(y_ps, 1)

            pe.wait_ge(plan_ready, 1)
            turn_in(0, 0, 0)
            up(0, 0, 0)
            turn_in(1, 1, 0)
            down(0, 0, 0)
            up(1, 1, 0)
            with pe.Fori(1, N_SLOT_TILES // 2) as k:
                turn_in(2 * k, 0, k)
                down(2 * k - 1, 1, k - 1)
                up(2 * k, 0, k)
                turn_in(2 * k + 1, 1, k)
                down(2 * k, 0, k)
                up(2 * k + 1, 1, k)
            down(N_SLOT_TILES - 1, 1, N_SLOT_TILES // 2 - 1)

        @block.scalar
        def _(act):
            S = nc.scalar
            act.wait_ge(wt_ps, 1)
            S.copy(attn_t[:], bank[2][0:F, 0:HEADS]).then_inc(wt_done, 1)
            S.copy(b1_t[:], bank[3][:, 0:EXPERTS * H_CHUNKS])
            for d in range(2):
                last = S.copy(wcat[:, :, d * HALF_ROW:d * HALF_ROW + F],
                              bank[d][:, 0:D_CHUNKS * F].rearrange("p (c f) -> p c f", c=D_CHUNKS))
            last.then_inc(at_done, 1)
            act.wait_ge(wt_ps, 2)
            for d in range(2):
                last = S.copy(wcat[:, :, d * HALF_ROW + F:(d + 1) * HALF_ROW],
                              bank[4][:, 2 * d * HEADS:2 * (d + 1) * HEADS].rearrange("p (c h) -> p c h", c=D_CHUNKS))
            last.then_inc(wt_done, 1)

            n = 0
            for _, target in turned:
                for half in range(2):
                    for q in range(2):
                        act.wait_ge(tr_ps, n + 1)
                        to = target[:, half * HALF_GROUPS * TILES:(half + 1) * HALF_GROUPS * TILES]
                        to = to.rearrange("p (r j) -> p r j", j=TILES)[:, :, 4 * q:4 * q + 4]
                        S.copy(to, bank[n % 2][:, 0:4 * HALF_GROUPS].rearrange("p (j r) -> p r j", j=4)).then_inc(tr_done, 1)
                        n += 1

            act.wait_ge(ln_var, 1)
            S.activation(ln_b[:], ln_a[:], ACT.Sqrt, bias=eps_t[:], scale=1.0 / D).then_inc(ln_std, 1)

            def out_turned(t, u, done=0, read=row_ps):
                act.wait_ge(xnt_ps, done + t + 1)
                at_least(act, read, t - 1)
                S.copy(xn_t[:, u, :], bank[2 + u][:, 0:D]).then_inc(xnt_ready, 1)

            def out_row(t, u, k):
                act.wait_ge(row_ps, t + 1)
                at_least(act, row_stored[u], 16 * k)
                S.copy(row_o[:, u, :], bank[6 + u][:, 0:ROW]).then_inc(row_ready, 1)

            for t in range(2):
                out_turned(t, t)
            out_row(0, 0, 0)
            with act.Fori(1, N_BLOCKS // 2) as k:
                out_turned(2 * k, 0)
                out_row(2 * k - 1, 1, k - 1)
                out_turned(2 * k + 1, 1)
                out_row(2 * k, 0, k)
            out_row(N_BLOCKS - 1, 1, N_BLOCKS // 2 - 1)

            def indices(g, u):
                S.copy(cur[:, u, :], src_t[:, cols(g * TILES, TILES)]).then_inc(idx_ready, 1)

            def products(g, u, k):
                act.wait_ge(gathered[u], (k + 1) * 16 * TILES)
                indices(g + 2, u)
                at_least(act, msg_ready, g - 1)
                for j in range(TILES):
                    for d in range(2):
                        part = slice(d * HALF_ROW, (d + 1) * HALF_ROW)
                        last = S.activation(prod[:, u, j, part], rows[:, u, j, part], ACT.Copy,
                                            scale=ea_t[:, d, cols(g * TILES + j, 1)])
                last.then_inc(prod_ready, 1)

            def weights(g, u):
                act.wait_ge(shifted_ready, g + 1)
                S.activation(wgt[:, u], shifted[:, u], ACT.Exp).then_inc(wgt_ready, 1)

            def rescale(g):
                act.wait_ge(dif_ready, g + 1)
                S.activation(alpha[:], m_dif[:], ACT.Exp).then_inc(alpha_ready, 1)

            indices(0, 0)
            indices(1, 1)
            products(0, 0, 0)
            products(1, 1, 0)
            weights(0, 0)
            with act.Fori(1, N_GROUPS // 2) as k:
                products(2 * k, 0, k)
                weights(2 * k - 1, 1)
                rescale(2 * k - 2)
                products(2 * k + 1, 1, k)
                weights(2 * k, 0)
                rescale(2 * k - 1)
            weights(N_GROUPS - 1, 1)
            rescale(N_GROUPS - 2)
            rescale(N_GROUPS - 1)

            act.wait_ge(guard_dif, 1)
            S.activation(alpha[:], m_dif[:], ACT.Exp).then_inc(guard_ready, 1)
            act.wait_ge(ln_var, 2)
            S.activation(ln_b[:], ln_a[:], ACT.Sqrt, bias=eps_t[:], scale=1.0 / D).then_inc(ln_std, 1)
            for t in range(2):
                out_turned(t, t, N_BLOCKS, gate_ps)
            with act.Fori(1, N_BLOCKS // 2) as k:
                for u in range(2):
                    out_turned(2 * k + u, u, N_BLOCKS, gate_ps)
            act.wait_ge(exp_in, 1)
            S.activation(prob, tmp_a, ACT.Exp).then_inc(exp_out, 1)

            def scatter_index(t, q, k):
                at_least(act, scattered[q], 32 * k)
                S.copy(slot_u[:, q, :], slot_i[:, cols(t, 1), :].rearrange("p o k -> p (o k)")).then_inc(slot_copied, 1)

            act.wait_ge(plan_ready, 1)
            for q in range(SCATTER_BUFS):
                scatter_index(q, q, 0)
            with act.Fori(1, N_FULL // SCATTER_BUFS) as k:
                for q in range(SCATTER_BUFS):
                    scatter_index(SCATTER_BUFS * k + q, q, k)
            scatter_index(N_FULL, 0, N_FULL // SCATTER_BUFS)

            def gelu(t, u):
                e = act.value_load(tile_i[0:1, cols(t, 1)], min_val=0, max_val=EXPERTS - 1)
                at_least(act, y_ps, t - 1)
                for c in range(H_CHUNKS):
                    if c % 2 == 0:
                        act.wait_ge(hid_ps, HID_BANKS * t + c // 2 + 1)
                    S.activation(hid[:, u, c, :], bank[2 + 2 * u + c // 2][:, (c % 2) * SLOT_TILE:(c % 2 + 1) * SLOT_TILE],
                                 ACT.Gelu, bias=b1_t[:, cols(e * H_CHUNKS + c, 1)]).then_inc(hid_ready, 1)

            def store_y(t, u):
                act.wait_ge(y_ready, t + 1)
                act.dma_start(slots_out[cols(t * SLOT_TILE, SLOT_TILE), :].rearrange("(s p) d -> p s d", p=P),
                              y_out[:, u].rearrange("p (s d) -> p s d", s=SUB)).then_inc(y_stored[u], 16)

            gelu(0, 0)
            gelu(1, 1)
            store_y(0, 0)
            with act.Fori(1, N_SLOT_TILES // 2) as k:
                gelu(2 * k, 0)
                store_y(2 * k - 1, 1)
                gelu(2 * k + 1, 1)
                store_y(2 * k, 0)
            store_y(N_SLOT_TILES - 1, 1)

            def fetch_index(t, u, k):
                at_least(act, y_fetched[u], 32 * k)
                S.copy(slot_u[:, u, :], slot_i[:, cols(t, 1), :].rearrange("p o k -> p (o k)")).then_inc(fetch_idx, 1)

            for q in range(SCATTER_BUFS):
                act.wait_ge(scattered[q], 32 * (N_FULL // SCATTER_BUFS + (q == 0)))
            for t in range(2):
                fetch_index(t, t, 0)
            with act.Fori(1, N_FULL // 2) as k:
                for u in range(2):
                    fetch_index(2 * k + u, u, k)
            fetch_index(N_FULL, 0, N_FULL // 2)

        @block.vector
        def _(dve):
            V = nc.vector
            links = [0]

            def link(ins):
                links[0] += 1
                ins.then_inc(setup_link, 1)
                dve.wait_ge(setup_link, links[0])

            dve.wait_ge(dst_loaded, 64)
            for half in range(2):
                part = dst_n[0:HALF_GROUPS, half * GROUP:(half + 1) * GROUP]
                V.tensor_reduce(blk_i[:, half:half + 1], part, AX.X, ALU.min)
                last = V.tensor_reduce(blk_i[:, 2 + half:3 + half], part, AX.X, ALU.max)
            link(last)
            link(V.tensor_scalar(blk_i[:], blk_i[:], 7, None, ALU.logical_shift_right))
            V.tensor_copy(blk_f[:], blk_i[:]).then_inc(blk_ready, 1)
            V.tensor_copy(dst_f[0:HALF_GROUPS, :], dst_n[0:HALF_GROUPS, :]).then_inc(dst_conv, 1)
            dve.wait_ge(src_loaded, 64)
            V.tensor_copy(src_f[0:HALF_GROUPS, :], src_n[0:HALF_GROUPS, :]).then_inc(src_conv, 1)
            dve.wait_ge(blkrow_ps, 1)
            V.tensor_copy(blk_row[:], bank[5][0:1, 0:2 * N_GROUPS]).then_inc(row_first, 1)
            dve.wait_ge(row_first, 1)
            first, final = blk_row[0:1, 0:N_GROUPS], blk_row[0:1, N_GROUPS:2 * N_GROUPS]
            V.tensor_copy(walk[0:1, 0, :], first)
            link(V.tensor_tensor(scan[0:1, 0, :], final, first, ALU.subtract))
            V.tensor_copy(walk[0:1, 1, :], scan[0:1, 0, :])
            link(V.tensor_scalar(scan[0:1, 1, 1:N_GROUPS], scan[0:1, 0, 0:N_GROUPS - 1], 1.0, 0.0, ALU.subtract, ALU.max))
            link(V.memset(scan[0:1, 1, 0:1], 0.0))
            at, step = 1, 1
            while step < N_GROUPS:
                V.tensor_copy(scan[0:1, 1 - at, 0:step], scan[0:1, at, 0:step])
                link(V.tensor_tensor(scan[0:1, 1 - at, step:], scan[0:1, at, step:], scan[0:1, at, 0:N_GROUPS - step], ALU.add))
                at, step = 1 - at, 2 * step
            V.tensor_copy(walk[0:1, 2, :], scan[0:1, at, :]).then_inc(walk_ready, 1)

            def ln_statistics():
                with dve.Fori(0, N_BLOCKS // 2) as k:
                    for u in range(2):
                        t = 2 * k + u
                        V.bn_stats(stats[:, cols(t, 1), :], xres[:, cols(t * D, D)])
                link(V.tensor_copy(ln_a[:, 0:1], eps_t[:]))
                link(V.tensor_tensor(mean[:], stats[:, :, 1], stats[:, :, 4], ALU.add))
                link(V.tensor_tensor(ln_a[:], stats[:, :, 1], stats[:, :, 4], ALU.subtract))
                link(V.tensor_scalar(mean[:], mean[:], 0.5, None, ALU.mult))
                link(V.tensor_tensor(ln_a[:], ln_a[:], ln_a[:], ALU.mult))
                link(V.tensor_tensor(ln_b[:], stats[:, :, 2], stats[:, :, 5], ALU.add))
                V.scalar_tensor_tensor(ln_a[:], ln_a[:], D / 4.0, ln_b[:], ALU.mult, ALU.add).then_inc(ln_var, 1)

            dve.wait_ge(x_loaded, 16)
            dve.wait_ge(x_tail_loaded, 16)
            dve.wait_ge(consts, 2)
            ln_statistics()
            dve.wait_ge(ln_std, 1)
            link(V.reciprocal(rstd[:], ln_b[:]))

            dve.wait_ge(tr_done, 8)
            dve.wait_ge(blkrow_ps, 2)
            d3 = dst_t[:].rearrange("p (g j) -> p g j", j=TILES)
            link(V.scalar_tensor_tensor(d3, bc(bank[6][:, 0:N_GROUPS].unsqueeze(2), [P, N_GROUPS, TILES]), -float(P),
                                        d3, ALU.mult, ALU.add))
            real = TAIL // P
            part = TAIL % P
            V.memset(dst_t[part:P, (N_GROUPS - 1) * TILES + real:(N_GROUPS - 1) * TILES + real + 1], LOWEST)
            V.memset(dst_t[:, (N_GROUPS - 1) * TILES + real + 1:], LOWEST).then_inc(edges_ready, 1)

            def normalise(t, u, done=0):
                at_least(dve, xnt_ps, done + t - 1)
                V.tensor_scalar(xn[:, u, :], xres[:, cols(t * D, D)], mean[:, cols(t, 1)], rstd[:, cols(t, 1)],
                                ALU.subtract, ALU.mult).then_inc(xn_ready, 1)

            for t in range(2):
                normalise(t, t)
            with dve.Fori(1, N_BLOCKS // 2) as k:
                for u in range(2):
                    normalise(2 * k + u, u)

            V.memset(acc[:], 0.0)
            V.memset(m_blk[:], LOWEST)
            link(V.memset(rmax[:], LOWEST))

            def messages(g, u):
                dve.wait_ge(prod_ready, g + 1)
                V.tensor_tensor(msg[:, u], prod[:, u, :, 0:HALF_ROW], prod[:, u, :, HALF_ROW:ROW], ALU.add).then_inc(msg_ready, 1)
                dve.wait_ge(msg_ready, g + 1)
                scores = msg[:, u, :, F:HALF_ROW]
                V.scalar_tensor_tensor(lrelu[:, u], scores, LEAK, scores, ALU.mult, ALU.max).then_inc(msg_link, 1)
                dve.wait_ge(msg_link, g + 1)
                V.tensor_reduce(gmax[:, u, :], lrelu[:, u].rearrange("p j h -> p h j"), AX.X, ALU.max).then_inc(gmax_ready, 1)

            def one_hots(g, u):
                at_least(dve, sums_ready, g - 1)
                d = bc(dst_t[:, cols(g * TILES, TILES)].unsqueeze(2), [P, TILES, P])
                V.tensor_tensor(onehot[:, u], bc(iota0[:].unsqueeze(1), [P, TILES, P]), d, ALU.is_equal)
                more = dve.value_load(walk[0:1, 1, cols(g, 1)], min_val=0, max_val=N_BLOCKS)
                with dve.If(more > 0):
                    V.tensor_tensor(onehot_x[:, u], bc(iota1[:].unsqueeze(1), [P, TILES, P]), d, ALU.is_equal)

            def weighted(g, u):
                dve.wait_ge(wgt_ready, g + 1)
                v4 = val[:, u].rearrange("p j (h c) -> p j h c", h=HEADS)
                V.tensor_copy(v4[:, :, :, F], wgt[:, u])
                V.tensor_tensor(v4[:, :, :, 0:F], bc(msg[:, u, :, 0:F].unsqueeze(2), [P, TILES, HEADS, F]),
                                bc(wgt[:, u].unsqueeze(3), [P, TILES, HEADS, F]), ALU.mult).then_inc(val_ready, 1)

            def maximum(g, u):
                dve.wait_ge(gmaxt_ready, g + 1)
                V.tensor_reduce(tmax[:], bank[4][0:HEADS, u * P:(u + 1) * P], AX.X, ALU.max).then_inc(max_link, 1)
                dve.wait_ge(max_link, 3 * g + 1)
                V.tensor_tensor(rmax[:, u:u + 1], rmax[:, 1 - u:2 - u], tmax[:], ALU.max).then_inc(max_link, 1)
                dve.wait_ge(max_link, 3 * g + 2)
                V.tensor_scalar(diag[:, u, :], ident[0:HEADS, 0:HEADS], rmax[:, u:u + 1], None, ALU.mult).then_inc(diag_ready, 1)
                dve.wait_ge(max_ready, g + 1)
                V.tensor_copy(m_all[:, cols(g, 1), :], bank[5][:, u * HEADS:(u + 1) * HEADS].unsqueeze(1)).then_inc(max_link, 1)
                dve.wait_ge(max_link, 3 * g + 3)
                V.tensor_tensor(shifted[:, u], lrelu[:, u], bc(m_all[:, cols(g, 1), :], [P, TILES, HEADS]),
                                ALU.subtract).then_inc(shifted_ready, 1)

            def add_block(b, g, from_bank):
                a = acc[:, cols(b * ACC, ACC)]
                a3 = a.rearrange("p (h c) -> p h c", h=HEADS)
                al = bc(alpha[:, cols(b, 1), :].rearrange("p o h -> p (o h)").unsqueeze(2), [P, HEADS, HEAD_COLS])
                V.tensor_tensor(a3, a3, al, ALU.mult)
                dve.drain()
                V.tensor_tensor(a, a, from_bank[:, 0:ACC], ALU.add)
                V.tensor_copy(m_blk[:, cols(b, 1), :], m_all[:, cols(g, 1), :])

            def accumulate(g, u):
                b = dve.value_load(walk[0:1, 0, cols(g, 1)], min_val=0, max_val=N_FULL)
                more = dve.value_load(walk[0:1, 1, cols(g, 1)], min_val=0, max_val=N_BLOCKS - 1)
                dve.wait_ge(sums_ready, g + 1)
                dve.wait_ge(alpha_ready, g + 1)
                add_block(b, g, bank[u])
                with dve.If(more > 0):
                    dve.drain()
                    add_block(b + 1, g, bank[2 + u])
                    dve.drain()
                    V.tensor_scalar(dst_k[:], dst_t[:, cols(g * TILES, TILES)], float(P), None, ALU.subtract)
                with dve.If(more > 1):
                    before = dve.value_load(walk[0:1, 2, cols(g, 1)], min_val=0, max_val=N_BLOCKS * N_GROUPS)
                    with dve.Fori(1, more) as k:
                        dve.drain()
                        V.tensor_scalar(dst_k[:], dst_k[:], float(P), None, ALU.subtract)
                        dve.drain()
                        V.tensor_tensor(onehot_x[:, u], bc(iota0[:].unsqueeze(1), [P, TILES, P]),
                                        bc(dst_k[:].unsqueeze(2), [P, TILES, P]), ALU.is_equal).then_inc(rest_ready, 1)
                        dve.wait_ge(rest_sums, before + k)
                        add_block(nc.s_assert_within(b + 1 + k, min_val=0, max_val=N_FULL, 
                                    skip_runtime_bounds_check_because="k stays below more, and first + more is the last block"), g, bank[6])
                dve.drain()

            def differences(g):
                V.tensor_tensor(m_dif[:], m_blk[:], bc(m_all[:, cols(g, 1), :], [P, N_BLOCKS, HEADS]),
                                ALU.subtract).then_inc(dif_ready, 1)

            def slot(g, u, first=True, second=True, third=True):
                if first:
                    messages(g, u)
                if second:
                    one_hots(g - 1, 1 - u)
                    weighted(g - 1, 1 - u)
                if first:
                    maximum(g, u)
                if third:
                    accumulate(g - 2, u)
                if second:
                    differences(g - 1)

            slot(0, 0, second=False, third=False)
            slot(1, 1, third=False)
            with dve.Fori(1, N_GROUPS // 2) as k:
                for u in range(2):
                    slot(2 * k + u, u)
            slot(N_GROUPS, 0, first=False)
            slot(N_GROUPS + 1, 1, first=False, second=False)
            V.tensor_copy(rmax[:, 0:1], rmax[:, 1:2]).then_inc(edges_done, 1)

            last_max = bc(m_all[:, N_GROUPS - 1:N_GROUPS, :], [P, N_BLOCKS, HEADS])
            link(V.tensor_tensor(m_dif[:], last_max, m_blk[:], ALU.subtract))
            V.tensor_scalar(m_dif[:], m_dif[:], GUARD_CAP, None, ALU.min).then_inc(guard_dif, 1)
            dve.wait_ge(guard_ready, 1)
            sums4 = acc[:].rearrange("p (t h c) -> p t h c", t=N_BLOCKS, h=HEADS)
            link(V.scalar_tensor_tensor(den[:], alpha[:], GUARD, sums4[:, :, :, F], ALU.mult, ALU.add))
            link(V.reciprocal(den[:], den[:]))
            heads3 = acc[:].rearrange("p (k c) -> p k c", c=HEAD_COLS)[:, :, 0:F]
            link(V.tensor_tensor(heads3, heads3,
                                 bc(den[:].rearrange("p t h -> p (t h)").unsqueeze(2), [P, N_BLOCKS * HEADS, F]), ALU.mult))
            x3 = xres[:].rearrange("p (k c) -> p k c", c=F)
            link(V.tensor_tensor(x3, x3, heads3, ALU.add))
            ln_statistics()
            dve.wait_ge(ln_std, 2)
            link(V.reciprocal(rstd[:], ln_b[:]))

            def logits(t, u):
                dve.wait_ge(gate_ps, t + 1)
                V.tensor_tensor(prob[:, cols(t, 1), :], bank[6 + u][:, 0:EXPERTS].unsqueeze(1), gb[:].unsqueeze(1),
                                ALU.add).then_inc(logit_ready, 1)

            for t in range(2):
                normalise(t, t, N_BLOCKS)
            with dve.Fori(1, N_BLOCKS // 2) as k:
                normalise(2 * k, 0, N_BLOCKS)
                logits(2 * k - 2, 0)
                normalise(2 * k + 1, 1, N_BLOCKS)
                logits(2 * k - 1, 1)
            logits(N_BLOCKS - 2, 0)
            logits(N_BLOCKS - 1, 1)
            dve.wait_ge(logit_ready, N_BLOCKS)

            full = [P, N_BLOCKS, EXPERTS]

            def spread(c):
                return bc(c.unsqueeze(2), full)

            experts = bc(iota0[:, 0:EXPERTS].unsqueeze(1), full)
            link(V.tensor_reduce(col[:, 0, :], prob, AX.X, ALU.max))
            V.tensor_tensor(tmp_a, prob, spread(col[:, 0, :]), ALU.subtract).then_inc(exp_in, 1)
            link(V.tensor_scalar(iota8, experts, float(EXPERTS), None, ALU.add))
            dve.wait_ge(exp_out, 1)
            link(V.tensor_reduce(col[:, 0, :], prob, AX.X, ALU.add))
            link(V.reciprocal(col[:, 1, :], col[:, 0, :]))
            link(V.tensor_tensor(prob, prob, spread(col[:, 1, :]), ALU.mult))
            for k, hot in enumerate((top_1, top_2)):
                link(V.tensor_reduce(weight[:, k, :], prob, AX.X, ALU.max))
                link(V.tensor_tensor(tmp_a, prob, spread(weight[:, k, :]), ALU.is_equal))
                link(V.scalar_tensor_tensor(tmp_b, tmp_a, -float(EXPERTS), iota8, ALU.mult, ALU.add))
                link(V.tensor_reduce(col[:, 2, :], tmp_b, AX.X, ALU.min))
                link(V.tensor_tensor(hot, experts, spread(col[:, 2, :]), ALU.is_equal))
                link(V.scalar_tensor_tensor(prob, hot, -2.0, prob, ALU.mult, ALU.add))
            link(V.tensor_tensor(both, top_1, top_2, ALU.add))
            V.memset(both[:, N_FULL + 1:N_BLOCKS, :], 0.0)
            V.tensor_scalar(both[:, N_FULL, :], both[:, N_FULL, :], valid[:], None, ALU.mult).then_inc(both_ready, 1)

            dve.wait_ge(rank_ps, 1)
            totals = bank[1][:, 0:BE].rearrange("p (t e) -> p t e", e=EXPERTS)
            link(V.tensor_copy(scan_a, totals))
            a, b, step = scan_a, scan_b, 1
            while step < N_BLOCKS:
                V.tensor_copy(b[:, 0:step, :], a[:, 0:step, :])
                link(V.tensor_tensor(b[:, step:, :], a[:, step:, :], a[:, 0:N_BLOCKS - step, :], ALU.add))
                a, b, step = b, a, 2 * step
            link(V.tensor_scalar(count_i[:], a[:, N_BLOCKS - 1, :], float(SLOT_TILE - 1), None, ALU.add))
            link(V.tensor_scalar(count_i[:], count_i[:], 8, None, ALU.logical_shift_right))
            link(V.tensor_copy(counts[:, 0, :], count_i[:]))
            link(V.tensor_copy(counts[:, 1, :], counts[:, 0, :]))
            p0, p1, step = 1, 2, 1
            while step < EXPERTS:
                V.tensor_copy(counts[:, p1, 0:step], counts[:, p0, 0:step])
                link(V.tensor_tensor(counts[:, p1, step:], counts[:, p0, step:], counts[:, p0, 0:EXPERTS - step], ALU.add))
                p0, p1, step = p1, p0, 2 * step
            link(V.tensor_tensor(counts[:, 3, :], counts[:, p0, :], counts[:, 0, :], ALU.subtract))
            link(V.tensor_scalar(counts[:, 3, :], counts[:, 3, :], float(SLOT_TILE), None, ALU.mult))
            link(V.tensor_tensor(tile_x, bc(iota0[0:1, 0:N_SLOT_TILES].unsqueeze(2), [1, N_SLOT_TILES, EXPERTS - 1]),
                                 bc(counts[0:1, p0, 0:EXPERTS - 1].unsqueeze(1), [1, N_SLOT_TILES, EXPERTS - 1]), ALU.is_ge))
            link(V.tensor_reduce(tile_e[:], tile_x, AX.X, ALU.add))
            V.tensor_copy(tile_i[:], tile_e[:])
            link(V.tensor_tensor(b, a, totals, ALU.subtract))
            link(V.tensor_tensor(b, b, bank[0][:, 0:BE].rearrange("p (t e) -> p t e", e=EXPERTS), ALU.add))
            link(V.tensor_tensor(b, b, bc(counts[:, 3, :].unsqueeze(1), full), ALU.add))
            for k, hot in enumerate((top_1, top_2)):
                link(V.tensor_tensor(tmp_a, b, hot, ALU.mult))
                link(V.tensor_reduce(col[:, k, :], tmp_a, AX.X, ALU.add))
                last = V.tensor_copy(slot_i[:, :, k], col[:, k, :])
            last.then_inc(plan_ready, 1)

            def token(t, q, k):
                at_least(dve, scattered[q], 32 * k)
                V.tensor_scalar(tok[:, q, :], xres[:, cols(t * D, D)], mean[:, cols(t, 1)], rstd[:, cols(t, 1)],
                                ALU.subtract, ALU.mult).then_inc(tok_ready, 1)

            for q in range(SCATTER_BUFS):
                token(q, q, 0)
            with dve.Fori(1, N_FULL // SCATTER_BUFS) as k:
                for q in range(SCATTER_BUFS):
                    token(SCATTER_BUFS * k + q, q, k)
            token(N_FULL, 0, N_FULL // SCATTER_BUFS)

            def in_turned(t, u):
                dve.wait_ge(xin_ps, t + 1)
                at_least(dve, hid_ps, HID_BANKS * (t - 1))
                V.tensor_copy(x_int[:, u, :], bank[u][:]).then_inc(xin_ready, 1)

            def add_b2(t, u, k):
                e = dve.value_load(tile_i[0:1, cols(t, 1)], min_val=0, max_val=EXPERTS - 1)
                dve.wait_ge(y_ps, t + 1)
                at_least(dve, y_stored[u], 16 * k)
                V.tensor_tensor(y_out[:, u].rearrange("p (s d) -> p s d", s=SUB),
                                bank[6 + u][:].rearrange("p (s d) -> p s d", s=SUB),
                                bc(b2_rep[:, cols(e * D, D)].unsqueeze(1), [P, SUB, D]), ALU.add).then_inc(y_ready, 1)

            dve.wait_ge(b2_loaded, 16)
            in_turned(0, 0)
            in_turned(1, 1)
            add_b2(0, 0, 0)
            with dve.Fori(1, N_SLOT_TILES // 2) as k:
                in_turned(2 * k, 0)
                add_b2(2 * k - 1, 1, k - 1)
                in_turned(2 * k + 1, 1)
                add_b2(2 * k, 0, k)
            add_b2(N_SLOT_TILES - 1, 1, N_SLOT_TILES // 2 - 1)

            def combine(t, u, k, n=P):
                dve.wait_ge(y_fetched[u], 32 * (k + 1))
                at_least(dve, res_stored[u], 16 * k)
                r = res[0:n, u, :]
                V.scalar_tensor_tensor(r, y_tok[0:n, u, 0, :], weight[0:n, 0, cols(t, 1)], xres[0:n, cols(t * D, D)],
                                       ALU.mult, ALU.add).then_inc(res_link, 1)
                dve.wait_ge(res_link, t + 1)
                V.scalar_tensor_tensor(r, y_tok[0:n, u, 1, :], weight[0:n, 1, cols(t, 1)], r,
                                       ALU.mult, ALU.add).then_inc(res_ready, 1)

            for t in range(2):
                combine(t, t, 0)
            with dve.Fori(1, N_FULL // 2) as k:
                for u in range(2):
                    combine(2 * k + u, u, k)
            combine(N_FULL, 0, N_FULL // 2, LAST)


_INS = ["x", "src", "dst", "edge_attr_2", "L0_gnn_W_forward", "L0_gnn_W_reverse", "L0_gnn_attn_forward",
        "L0_ffn_gate_w", "L0_ffn_gate_b", "L0_ffn_W1", "L0_ffn_b1", "L0_ffn_W2", "L0_ffn_b2"]


def kernel(**inputs):
    import numpy as np
    import concourse.bacc as bacc
    from concourse.bass_utils import run_bass_kernel_spmd

    nc = bacc.Bacc("TRN2", target_bir_lowering=False, num_devices=1)
    arrays, args = {}, []
    for name in _INS:
        a = np.ascontiguousarray(inputs[name])
        arrays[f"in_{name}"] = a
        args.append(nc.dram_tensor(f"in_{name}", a.shape, mybir.dt.from_np(a.dtype), kind="ExternalInput").ap())
    out = nc.dram_tensor("out", (N_NODES, D), F32, kind="ExternalOutput").ap()
    build(nc, *args, out)
    r = run_bass_kernel_spmd(nc, [arrays], core_ids=[0])
    return r.results[0]["out"]
```
